# Optimizing a Trainium2 kernel written in Bass

```python
import numpy as np
import jax
import jax.numpy as jnp

def _softmax(x, axis=-1):
    return jax.nn.softmax(x, axis=axis)

def _gelu(x):
    return jax.nn.gelu(x, approximate=True)

def _silu(x):
    return jax.nn.silu(x)

def _sigmoid(x):
    return jax.nn.sigmoid(x)

def _layernorm(x, axis=-1, eps=1e-05):
    m = jnp.mean(x, axis=axis, keepdims=True)
    v = jnp.var(x, axis=axis, keepdims=True)
    return (x - m) / jnp.sqrt(v + eps)

def _scatter_add(tgt, idx, src, axis=0):
    return tgt.at[idx].add(src)

def _segment_sum(src, seg, n):
    return jax.ops.segment_sum(src, seg, n)
kernel_name = 'mk_seq_postln_d1_jaxref_r8_6747b6'

def setup_inputs(seed: int=0):
    np.random.seed(seed)
    _w = jnp.asarray

    def _L0_attn_setup():
        import jax, jax.numpy as jnp
        import numpy as np
        B, S, D_MODEL, H, D = (2, 256, 128, 16, 64)
        SCALE = 1.0 / float(np.sqrt(D))

        def _rope(t, c, s):
            d2 = t.shape[-1] // 2
            t1, t2 = (t[..., :d2], t[..., d2:])
            return jnp.concatenate([t1 * c - t2 * s, t1 * s + t2 * c], axis=-1)
        key = jax.random.key(seed)
        ks = jax.random.split(key, 5)
        x = jax.random.normal(ks[0], (B, S, D_MODEL), jnp.float32)
        qkv_w = jax.random.normal(ks[1], (3 * H * D, D_MODEL), jnp.float32) * 0.02
        out_w = jax.random.normal(ks[2], (D_MODEL, H * D), jnp.float32) * 0.02
        bias_p = jax.random.uniform(ks[3], (H, 1, 1), jnp.float32) * 2.0
        bias_a = jax.random.uniform(ks[4], (H, 1, 1), jnp.float32)
        rope_freqs = 10000.0 ** (-jnp.arange(D // 2, dtype=jnp.float32) / (D // 2))
        return {'x': x, 'qkv_w': qkv_w, 'out_w': out_w, 'bias_p': bias_p, 'bias_a': bias_a, 'rope_freqs': rope_freqs}
    _L0_attn_in = _L0_attn_setup()

    def _L0_ffn_setup():
        import jax, jax.numpy as jnp
        import numpy as np
        key = jax.random.key(seed)
        kx, kw = jax.random.split(key)
        x = jax.random.normal(kx, (32, 512, 128), dtype=jnp.float32)
        weight = jax.random.normal(kw, (128, 128), dtype=jnp.float32) * 0.01
        return {'x': x, 'weight': weight}
    _L0_ffn_in = _L0_ffn_setup()
    _d = {'L0_attn_x': _L0_attn_in['x'], 'L0_attn_qkv_w': _L0_attn_in['qkv_w'], 'L0_attn_out_w': _L0_attn_in['out_w'], 'L0_attn_bias_p': _L0_attn_in['bias_p'], 'L0_attn_bias_a': _L0_attn_in['bias_a'], 'L0_attn_rope_freqs': _L0_attn_in['rope_freqs'], 'L0_ffn_weight': _L0_ffn_in['weight']}
    _x0 = _d['L0_attn_x']
    _d['L0_attn_x'] = jax.random.normal(jax.random.fold_in(jax.random.key(seed), 1), (1, 2048, 128), dtype=_x0.dtype)
    del _x0
    return _d

def reference(L0_attn_x, L0_attn_qkv_w, L0_attn_out_w, L0_attn_bias_p, L0_attn_bias_a, L0_attn_rope_freqs, L0_ffn_weight):

    def _L0_attn_ref(x, qkv_w, out_w, bias_p, bias_a, rope_freqs):
        import jax, jax.numpy as jnp
        import numpy as np
        B, S, D_MODEL, H, D = (2, 256, 128, 16, 64)
        SCALE = 1.0 / float(np.sqrt(D))

        def _rope(t, c, s):
            d2 = t.shape[-1] // 2
            t1, t2 = (t[..., :d2], t[..., d2:])
            return jnp.concatenate([t1 * c - t2 * s, t1 * s + t2 * c], axis=-1)
        Bb, Ss, _ = x.shape
        qkv = (x @ qkv_w.T).reshape(Bb, Ss, 3, H, D)
        q = qkv[:, :, 0].transpose(0, 2, 1, 3)
        k = qkv[:, :, 1].transpose(0, 2, 1, 3)
        v = qkv[:, :, 2].transpose(0, 2, 1, 3)
        pos = jnp.arange(Ss, dtype=jnp.float32)
        ang = pos[:, None] * rope_freqs[None, :]
        c = jnp.cos(ang)[None, None]
        s = jnp.sin(ang)[None, None]
        q = _rope(q, c, s)
        k = _rope(k, c, s)
        scores = jnp.einsum('bhqd,bhkd->bhqk', q, k) * SCALE
        p = jnp.maximum(bias_p, 0.01)
        a = jnp.maximum(bias_a, 0.01)
        dist = jnp.abs(pos[None, :] - pos[:, None])
        kb = -p * jnp.log1p(a * dist)
        attn = jax.nn.softmax(scores + kb[None], axis=-1)
        out = jnp.einsum('bhqk,bhkd->bhqd', attn, v)
        out = out.transpose(0, 2, 1, 3).reshape(Bb, Ss, H * D)
        return out @ out_w.T

    def _L0_ffn_ref(x, weight):
        import jax, jax.numpy as jnp
        import numpy as np
        b_weight = jnp.sign(weight)
        return jnp.einsum('bsi,oi->bso', x, b_weight)
    x = L0_attn_x
    x = _layernorm(x + _L0_attn_ref(x, L0_attn_qkv_w, L0_attn_out_w, L0_attn_bias_p, L0_attn_bias_a, L0_attn_rope_freqs), axis=-1)
    x = _layernorm(x + _L0_ffn_ref(x, L0_ffn_weight), axis=-1)
    return x

_drawn_inputs = setup_inputs


def setup_inputs(seed=0):
    import zlib

    import numpy as np

    out = dict(_drawn_inputs(seed))
    spreads = {}
    factors = {'L0_attn_bias_p': 3.167, 'L0_attn_bias_a': 3.833, 'L0_attn_rope_freqs': 8.0}
    for name, (base, spread) in spreads.items():
        noise = np.random.default_rng([zlib.crc32(name.encode()), seed]).standard_normal(out[name].shape)
        drawn = base * np.exp(spread * noise) if base else spread * noise
        out[name] = jnp.asarray(drawn.astype(out[name].dtype))
    for name, factor in factors.items():
        out[name] = (out[name] * factor).astype(out[name].dtype)
    return out
```

```python
from contextlib import ExitStack

import numpy as np

import concourse.bass as bass
from concourse import mybir

F32 = mybir.dt.float32
F32R = mybir.dt.float32r
ALU = mybir.AluOpType
ACT = mybir.ActivationFunctionType

P = 128
S = 2048
DM = 128
H = 16
D = 64
NT = S // P
NPAIR = H // 2
TILES = 2 * NT
HALF = S // 2
TOE = S + S - P
ROW = 2 * S
SCALE = 1.0 / float(np.sqrt(D))
EPS = 1e-5
BIG = 3.0e38
RING = 4

CHUNK_TILE = {2: 0, 3: 1, 4: 2, 5: 3, 6: 4, 7: 5, 8: 6, 9: 7, 18: 8, 19: 9, 20: 10, 21: 11}
CHUNKS = 12
ROPE_STEPS = 5
STACKS = 6

ROUND = 1.5 * 2.0 ** 23
ROUND_HI = 1.5 * 2.0 ** 34
INV_2PI = float(np.float32(1.0 / (2.0 * np.pi)))


def two_pi_parts():
    rest, parts = 2.0 * np.pi, []
    for _ in range(3):
        unit = 2.0 ** (np.floor(np.log2(rest)) - 10)
        parts.append(float(np.floor(rest / unit) * unit))
        rest -= parts[-1]
    return parts, float(np.float32(rest))


def layer(nc, xT, x, wqkvT, owT, bias_p, bias_a, freqs, ffnT, out, rows, o_dram):
    with ExitStack() as ctx:
        def sb(name, shape, dt=F32):
            return ctx.enter_context(nc.sbuf_tensor(name, shape, dt))

        def psum(name, shape):
            return ctx.enter_context(nc.psum_tensor(name, shape, F32))

        def sem(name):
            return ctx.enter_context(nc.semaphore(name))

        xT_sb = sb("xT_sb", [P, S])
        w_sb = sb("w_sb", [P, 3, P])
        cos_t = sb("cos_t", [P, S])
        sin_t = sb("sin_t", [P, S])
        raw = [sb("raw_q", [P, S]), sb("raw_k", [P, S])]
        rot = sb("rot", [P, S])
        hi = [sb("hi_q", [P, S], F32R), sb("hi_k", [P, S], F32R)]
        lo = [sb("lo_q", [P, S], F32R), sb("lo_k", [P, S], F32R)]
        q_hl = [sb(f"q_hl{h}", [P, S], F32R) for h in range(2)]
        q_lh = [sb(f"q_lh{h}", [P, S], F32R) for h in range(2)]
        k_hl = [sb(f"k_hl{h}", [P, S], F32R) for h in range(2)]
        toe = [sb(f"toe{h}", [P, TOE]) for h in range(2)]
        v_sb = [sb(f"v{h}", [P, NT, D]) for h in range(2)]
        v_next = sb("v_next", [P, NT, D])
        prob = [sb(f"prob{b}", [P, S]) for b in range(2)]
        pT = sb("pT", [P, 4, 4, P])
        ident = sb("ident", [P, P])
        neg_max_h = sb("neg_max_h", [P, 2, 2])
        neg_max = sb("neg_max", [P, 2])
        row_sum = sb("row_sum", [P, RING])
        inv_sum = sb("inv_sum", [P, RING])
        o_norm = sb("o_norm", [P, RING, D])
        freq_c = sb("freq_c", [P, 1])
        a_c = sb("a_c", [H, 1])
        p_c = sb("p_c", [H, 1])

        sc_ps = psum("sc_ps", [P, 4, 512])
        tr_ps = [psum(f"tr_ps{b}", [P, 4, P]) for b in range(2)]
        o_ps = psum("o_ps", [P, 512])
        pj_ps = psum("pj_ps", [P, 512])

        W = S // 4
        ang, turns, t_hi, t_lo = (prob[0][:, n * W:n * W + W] for n in range(4))
        pos, sin_q, nsin_q, cos_q = (prob[1][:, n * W:n * W + W] for n in range(4))
        half_s = raw[1][:, 0:W]
        bias_row = [toe[b][0:H, 0:S] for b in range(2)]

        o_all = [prob[b][:, 0:H * D] for b in range(2)]
        oT = raw[0][:, :].rearrange("p (b c q) -> p b c q", b=2, c=8)
        y_fin = raw[1][:, :].rearrange("p (t d) -> p t d", t=NT)
        x_res = rot[:, :].rearrange("p (t d) -> p t d", t=NT)
        ow_sb = cos_t[:, 0:H * D].rearrange("p (c d) -> p c d", c=8)
        fw_raw, sgn, sgn_neg = (cos_t[:, H * D + n * P:H * D + n * P + P] for n in range(3))
        x1T = cos_t[:, 1536:1536 + 2 * P].rearrange("p (b q) -> p b q", b=2)
        x1 = sin_t[:, :].rearrange("p (t d) -> p t d", t=NT)
        stats, mean_var, std, inv_std = (cos_t[:, 1920 + 16 * n:1920 + 16 * n + w] for n, w in enumerate((6, 2, 1, 1)))

        x_in = sem("x_in")
        w_in = sem("w_in")
        small_in = sem("small_in")
        consts = sem("consts")
        dve_step = sem("dve_step")
        angles = sem("angles")
        params = sem("params")
        sines = sem("sines")
        tables = sem("tables")
        tab_in = sem("tab_in")
        logs = sem("logs")
        rows_done = sem("rows_done")
        rows_out = sem("rows_out")
        toe_in = [sem(f"toe_in{h}") for h in range(2)]
        stack_in = [sem(f"stack_in{h}") for h in range(2)]
        rot_in = sem("rot_in")
        rope_step = sem("rope_step")
        v_moved = sem("v_moved")
        proj_done = sem("proj_done")
        proj_out = sem("proj_out")
        scored = sem("scored")
        biased = sem("biased")
        max_done = sem("max_done")
        exp_done = sem("exp_done")
        transposed = sem("transposed")
        evac_act = sem("evac_act")
        evac_dve = sem("evac_dve")
        pv_done = sem("pv_done")
        inv_done = sem("inv_done")
        normed = sem("normed")
        o_out = [sem(f"o_out{s}") for s in range(RING)]
        fin_in = sem("fin_in")
        o_in = [sem(f"o_in{b}") for b in range(2)]
        o_tr = sem("o_tr")
        oT_out = sem("oT_out")
        attn_done = sem("attn_done")
        x1_done = sem("x1_done")
        x1_tr = sem("x1_tr")
        x1T_out = sem("x1T_out")
        sign_done = sem("sign_done")
        ffn_done = sem("ffn_done")
        fin_step = sem("fin_step")
        var_done = sem("var_done")
        std_done = sem("std_done")
        y_done = sem("y_done")
        y_out = sem("y_out")

        def is_first(pair):
            return isinstance(pair, int) and pair == 0

        def place(pair, t):
            pair, t = pair + t // TILES, t % TILES
            return pair, t, t // NT, t % NT

        def ready(eng, value):
            return value if isinstance(value, int) else eng.to_reg(value)

        block = ctx.enter_context(nc.Block())

        @block.sync
        def _(sp):
            for b in range(4):
                sp.dma_start(freq_c[32 * b:32 * b + 32], freqs[:, :]).then_inc(small_in, 16)
            sp.dma_start(a_c[:], bias_a[:, :]).then_inc(small_in, 16)
            sp.dma_start(p_c[:], bias_p[:, :]).then_inc(small_in, 16)
            sp.dma_start(w_sb[:], wqkvT[:, :, 0:P]).then_inc(w_in, 16)
            sp.dma_start(xT_sb[:], xT[:, :]).then_inc(x_in, 16)

            def rotate(pair, x):
                n_out = ready(sp, pair * CHUNKS + 4 * x + 4)
                n_summed = ready(sp, (pair * 2 + x) * ROPE_STEPS - 2)
                sp.wait_ge(proj_out, n_out)
                if not (is_first(pair) and x == 0):
                    sp.wait_ge(rope_step, n_summed)
                for a in range(4):
                    b = a ^ 1
                    sp.dma_start(rot[32 * a:32 * a + 32], raw[x][32 * b:32 * b + 32]).then_inc(rot_in, 16)

            def stack(pair, h):
                n_split = ready(sp, pair * 2 * ROPE_STEPS + 2 * ROPE_STEPS)
                n_biased = ready(sp, (pair - 1) * 2 * TILES + 2 * NT * (h + 1))
                sp.wait_ge(rope_step, n_split)
                if not is_first(pair):
                    sp.wait_ge(biased, n_biased)
                r = slice(D * h, D * h + D)
                for dst, src in ((q_hl[h][0:D], hi[0]), (q_hl[h][D:P], lo[0]), (q_lh[h][0:D], lo[0]),
                                 (q_lh[h][D:P], hi[0]), (k_hl[h][0:D], hi[1]), (k_hl[h][D:P], lo[1])):
                    sp.dma_start(dst.bitcast(F32), src[r].bitcast(F32)).then_inc(stack_in[h], 16)

            def toeplitz(pair, h):
                n = 2 * pair + h
                row = rows[n:n + 1, :] if isinstance(pair, int) else rows[bass.ds(n, 1), :]
                sp.dma_start(toe[h][:], bass.AP(tensor=row.tensor, offset=row.offset,
                                                ap=[[1, P], [1, TOE]])).then_inc(toe_in[h], 16)

            def store(j, t):
                _, _, h, i = place(j, t)
                cols = slice(j * P + h * D, j * P + h * D + D) if isinstance(j, int) else bass.ds(j * P + h * D, D)
                n_normed = ready(sp, j * TILES + t + 1)
                sp.wait_ge(x_in, 16)
                sp.wait_ge(normed, n_normed)
                sp.dma_start(o_dram[i * P:(i + 1) * P, cols], o_norm[:, t % RING, :]).then_inc(o_out[t % RING], 16)

            sp.wait_ge(tables, 2)
            for a in range(4):
                for b in range(4):
                    sp.dma_start(cos_t[32 * a:32 * a + 32, W * b:W * b + W],
                                 cos_q[32 * b:32 * b + 32]).then_inc(tab_in, 16)
                    sp.dma_start(sin_t[32 * a:32 * a + 32, W * b:W * b + W],
                                 (nsin_q if a % 2 == 0 else sin_q)[32 * b:32 * b + 32]).then_inc(tab_in, 16)
            rotate(0, 0)
            sp.wait_ge(rows_done, 2)
            for b in range(2):
                sp.dma_start(rows[:, b * S:b * S + S], bias_row[b]).then_inc(rows_out, 16)
            sp.wait_ge(rows_out, 32)
            toeplitz(0, 0)
            rotate(0, 1)
            stack(0, 0)
            stack(0, 1)
            toeplitz(0, 1)

            def body(j, last):
                for t in range(TILES):
                    if last and t == 2:
                        sp.wait_ge(rope_step, NPAIR * 2 * ROPE_STEPS)
                        sp.dma_start(ow_sb, owT[:, :, :]).then_inc(fin_in, 16)
                        sp.dma_start(fw_raw, ffnT[:, :]).then_inc(fin_in, 16)
                        sp.dma_start(x_res, x[0].rearrange("(t p) d -> p t d", p=P)).then_inc(fin_in, 16)
                    if not last and t == 0:
                        n_proj = ready(sp, j * CHUNKS + CHUNKS)
                        sp.wait_ge(x_in, 16)
                        sp.wait_ge(proj_done, n_proj)
                        sp.dma_start(w_sb[:], wqkvT[:, :, bass.ds(j * P + P, P)]).then_inc(w_in, 16)
                    if not last and t == 7:
                        rotate(j + 1, 0)
                    if not last and t == 12:
                        rotate(j + 1, 1)
                    if not last and t == NT + 3:
                        stack(j + 1, 0)
                        toeplitz(j + 1, 0)
                    if t >= 1:
                        store(j, t - 1)
                if not last:
                    stack(j + 1, 1)
                    toeplitz(j + 1, 1)
                store(j, TILES - 1)

            body(0, False)
            with sp.Fori(1, NPAIR - 1) as j:
                body(j, False)
            body(NPAIR - 1, True)

            for s in range(RING):
                sp.wait_ge(o_out[s], 16 * H * NT // RING)
            for i in range(NT):
                if i >= 2:
                    sp.wait_ge(o_tr, 2 * (i - 2) + 2)
                sp.dma_start(o_all[i % 2], o_dram[i * P:(i + 1) * P, :]).then_inc(o_in[i % 2], 16)
            sp.wait_ge(y_done, NT)
            sp.dma_start(out[0].rearrange("(t p) d -> p t d", p=P), y_fin).then_inc(y_out, 16)
            sp.wait_ge(y_out, 16)

        @block.gpsimd
        def _(pool):
            made = [0]

            def make(ins):
                made[0] += 1
                ins.then_inc(consts, 1)
                pool.wait_ge(consts, made[0])

            exact = dict(channel_multiplier=0, allow_small_or_imprecise_dtypes=True)
            for b in range(4):
                make(nc.gpsimd.iota(pos[32 * b:32 * b + 32], pattern=[[1, W]], base=W * b, **exact))
            make(nc.gpsimd.iota(bias_row[0], pattern=[[-1, S]], base=S - 1, **exact))
            make(nc.gpsimd.iota(bias_row[1], pattern=[[1, S]], base=1, **exact))
            make(nc.gpsimd.memset(ident[:], 0.0))
            make(nc.gpsimd.affine_select(out=ident[:], in_=ident[:], compare_op=ALU.not_equal, fill=1.0, base=0,
                                         pattern=[[-1, P]], channel_multiplier=1))
            pool.wait_ge(tab_in, 32 * 16)

            def rope_split(pair, x):
                base = (pair * 2 + x) * ROPE_STEPS
                pool.wait_ge(proj_out, pair * CHUNKS + 4 * x + 4)
                pool.wait_ge(rot_in, (pair * 2 + x) * 64 + 64)
                nc.gpsimd.tensor_tensor(raw[x][:], raw[x][:], cos_t[:], ALU.mult).then_inc(rope_step, 1)
                nc.gpsimd.tensor_tensor(rot[:], rot[:], sin_t[:], ALU.mult).then_inc(rope_step, 1)
                pool.wait_ge(rope_step, base + 2)
                nc.gpsimd.tensor_tensor(raw[x][:], raw[x][:], rot[:], ALU.add).then_inc(rope_step, 1)
                n_summed = ready(pool, base + 3)
                n_stacked = ready(pool, pair * STACKS * 16)
                pool.wait_ge(tab_in, 32 * 16)
                pool.wait_ge(rope_step, n_summed)
                if not is_first(pair):
                    for h in range(2):
                        pool.wait_ge(stack_in[h], n_stacked)
                nc.gpsimd.tensor_copy(hi[x][:], raw[x][:]).then_inc(rope_step, 1)
                pool.wait_ge(rope_step, base + 4)
                nc.gpsimd.tensor_tensor(lo[x][:], raw[x][:], hi[x][:].bitcast(F32),
                                        ALU.subtract).then_inc(rope_step, 1)

            def move_v(pair):
                n_out = ready(pool, pair * CHUNKS + CHUNKS)
                n_pv = ready(pool, pair * 4 * TILES)
                pool.wait_ge(tab_in, 32 * 16)
                pool.wait_ge(proj_out, n_out)
                if not is_first(pair):
                    pool.wait_ge(pv_done, n_pv)
                nc.gpsimd.tensor_copy(v_sb[1][:], v_next[:]).then_inc(v_moved, 1)

            rope_split(0, 0)
            rope_split(0, 1)
            move_v(0)
            for x in range(2):
                rope_split(1, x)
            move_v(1)
            with pool.Fori(1, NPAIR - 1) as j:
                for x in range(2):
                    rope_split(j + 1, x)
                move_v(j + 1)

        @block.tensor
        def _(pe):
            def project(pair, c):
                if c == 0:
                    pe.wait_ge(w_in, pair * 16 + 16)
                if not (is_first(pair) and c == 0):
                    pe.wait_ge(proj_out, pair * CHUNKS + c)
                if c < 8:
                    s0 = (c % 4) * 512
                    mm = nc.tensor.matmul(pj_ps[:], w_sb[:, c // 4, :], xT_sb[:, s0:s0 + 512], start=True, stop=True)
                else:
                    for n in range(4):
                        s0 = ((c - 8) * 4 + n) * P
                        mm = nc.tensor.matmul(pj_ps[:, n * P:n * P + P], xT_sb[:, s0:s0 + P], w_sb[:, 2, :],
                                              start=True, stop=True)
                mm.then_inc(proj_done, 1)

            def score(j, t, half):
                pair, t, h, i = place(j, t)
                if i == 0 and half == 0:
                    pe.wait_ge(stack_in[h], pair * STACKS * 16 + STACKS * 16)
                if not (is_first(pair) and t == 0):
                    pe.wait_ge(biased, pair * 2 * TILES + 2 * t + half - 1)
                for n, q in enumerate((q_hl[h], q_lh[h])):
                    for b in (2 * half, 2 * half + 1):
                        mm = nc.tensor.matmul(sc_ps[:, b], q[:, i * P:i * P + P], k_hl[h][:, b * 512:b * 512 + 512],
                                              start=(n == 0), stop=(n == 1))
                mm.then_inc(scored, 1)

            def transpose(j, t, g):
                if g == 0:
                    pe.wait_ge(exp_done, j * TILES + t + 1)
                before = (evac_dve, evac_act, evac_act, evac_dve)[g]
                if not (is_first(j) and t == 0 and g < 2):
                    pe.wait_ge(before, j * 2 * TILES + 2 * t + (g >= 2))
                for n in range(4):
                    k0 = (4 * g + n) * P
                    mm = nc.tensor.transpose(tr_ps[g % 2][:, n, :], prob[t % 2][:, k0:k0 + P], ident[:])
                mm.then_inc(transposed, 1)

            def values(j, t, g):
                h = t // NT
                pe.wait_ge(evac_act if g in (0, 3) else evac_dve, j * 2 * TILES + 2 * t + 1 + (g >= 2))
                if t == 0 and g == 0:
                    pe.wait_ge(proj_out, j * CHUNKS + CHUNKS)
                if t == NT and g == 0:
                    pe.wait_ge(v_moved, j + 1)
                if g == 0 and not (is_first(j) and t == 0):
                    pe.wait_ge(normed, j * TILES + t)
                for n in range(4):
                    mm = nc.tensor.matmul(o_ps[:, 0:D], pT[:, g, n, :], v_sb[h][:, 4 * g + n, :],
                                          start=(g == 0 and n == 0), stop=(g == 3 and n == 3))
                mm.then_inc(pv_done, 1)

            pe.wait_ge(x_in, 16)
            for c in range(CHUNKS):
                project(0, c)
            pe.wait_ge(consts, 8)
            for t in range(2):
                for half in range(2):
                    score(0, t, half)

            def body(j, last):
                for t in range(TILES):
                    for g in range(2):
                        transpose(j, t, g)
                        if t >= 1:
                            values(j, t - 1, 2 + g)
                    if not last and t in CHUNK_TILE:
                        project(j + 1, CHUNK_TILE[t])
                    for g in range(2):
                        transpose(j, t, 2 + g)
                        if t + 2 < TILES or not last:
                            score(j, t + 2, g)
                        values(j, t, g)
                for g in range(2):
                    values(j, TILES - 1, 2 + g)

            body(0, False)
            with pe.Fori(1, NPAIR - 1) as j:
                body(j, False)
            body(NPAIR - 1, True)

            def o_transpose(i):
                pe.wait_ge(o_in[i % 2], 16 * (i // 2) + 16)
                if i >= 1:
                    pe.wait_ge(oT_out, 2 * i)
                for g in range(2):
                    for n in range(4):
                        c = 4 * g + n
                        mm = nc.tensor.transpose(tr_ps[g][:, n, :], o_all[i % 2][:, c * P:c * P + P], ident[:])
                    mm.then_inc(o_tr, 1)

            pe.wait_ge(fin_in, 48)
            pe.wait_ge(normed, NPAIR * TILES)
            o_transpose(0)
            for i in range(NT + 1):
                if i < NT:
                    pe.wait_ge(oT_out, 2 * i + 2)
                    if i >= 1:
                        pe.wait_ge(x1_done, i)
                    for c in range(8):
                        mm = nc.tensor.matmul(o_ps[:, 0:P], oT[:, i % 2, c, :], ow_sb[:, c, :],
                                              start=(c == 0), stop=(c == 7))
                    mm.then_inc(attn_done, 1)
                if i >= 1:
                    pe.wait_ge(x1_done, i)
                    if i >= 2:
                        pe.wait_ge(x1T_out, i - 1)
                    nc.tensor.transpose(pj_ps[:, 0:P], x1[:, i - 1, :], ident[:]).then_inc(x1_tr, 1)
                if i + 1 < NT:
                    o_transpose(i + 1)
                if i >= 1:
                    if i == 1:
                        pe.wait_ge(sign_done, 1)
                    pe.wait_ge(x1T_out, i)
                    if i >= 3:
                        pe.wait_ge(y_done, i - 2)
                    nc.tensor.matmul(sc_ps[:, (i - 1) % 2, 0:P], x1T[:, (i - 1) % 2, :], sgn,
                                     start=True, stop=True).then_inc(ffn_done, 1)

        @block.vector
        def _(dve):
            vec = nc.vector
            steps = {dve_step: 0, fin_step: 0}

            def chain(ins, on):
                steps[on] += 1
                ins.then_inc(on, 1)
                dve.wait_ge(on, steps[on])

            parts, rest = two_pi_parts()
            dve.wait_ge(consts, 4)
            dve.wait_ge(small_in, 96)
            chain(vec.tensor_scalar(ang, pos, freq_c[:, 0:1], None, ALU.mult), dve_step)
            chain(vec.tensor_scalar(t_hi, ang, INV_2PI, ROUND, ALU.mult, ALU.add), dve_step)
            chain(vec.tensor_scalar(turns, t_hi, ROUND, None, ALU.subtract), dve_step)
            chain(vec.tensor_scalar(t_hi, turns, ROUND_HI, ROUND_HI, ALU.add, ALU.subtract), dve_step)
            chain(vec.tensor_tensor(t_lo, turns, t_hi, ALU.subtract), dve_step)
            for part in parts:
                for n in (t_hi, t_lo):
                    chain(vec.scalar_tensor_tensor(out=ang, in0=n, scalar=-part, in1=ang, op0=ALU.mult, op1=ALU.add),
                          dve_step)
            chain(vec.scalar_tensor_tensor(out=ang, in0=turns, scalar=-rest, in1=ang, op0=ALU.mult, op1=ALU.add),
                  dve_step)
            vec.tensor_scalar(ang, ang, 3.1415925, -3.1415925, ALU.min, ALU.max).then_inc(angles, 1)
            vec.tensor_scalar(a_c[:], a_c[:], 0.01, None, ALU.max).then_inc(params, 1)
            vec.tensor_scalar(p_c[:], p_c[:], 0.01, None, ALU.max).then_inc(params, 1)
            dve.wait_ge(sines, 2)
            chain(vec.tensor_tensor(half_s, half_s, half_s, ALU.mult), dve_step)
            vec.tensor_scalar(cos_q, half_s, -2.0, 1.0, ALU.mult, ALU.add).then_inc(tables, 1)
            vec.tensor_scalar(nsin_q, sin_q, -1.0, None, ALU.mult).then_inc(tables, 1)
            dve.wait_ge(params, 2)
            for b in range(2):
                dve.wait_ge(logs, b + 1)
                vec.tensor_scalar(bias_row[b], bias_row[b], p_c[:, 0:1], None, ALU.mult).then_inc(rows_done, 1)
            def bias(j, t, half):
                pair, t, h, i = place(j, t)
                n_scored = ready(dve, pair * 2 * TILES + 2 * t + half + 1)
                n_toe = ready(dve, pair * 16 + 16) if i == 0 and half == 0 else None
                n_transposed = ready(dve, pair * 4 * TILES + 4 * (t - 2) + 2 * half + 2)
                dve.wait_ge(tab_in, 32 * 16)
                if i == 0 and half == 0:
                    dve.wait_ge(toe_in[h], n_toe)
                dve.wait_ge(scored, n_scored)
                if not (is_first(pair) and t < 2):
                    dve.wait_ge(transposed, n_transposed)
                c0 = P * i + S - HALF * (half + 1)
                vec.tensor_tensor_reduce(prob[t % 2][:, HALF * half:HALF * half + HALF],
                                         sc_ps[:, 2 * half:2 * half + 2].rearrange("p a b -> p (a b)"),
                                         toe[h][:, c0:c0 + HALF][:, ::-1], 1.0, BIG, ALU.add, ALU.min,
                                         neg_max_h[:, t % 2, half:half + 1]).then_inc(biased, 1)

            def maximum(j, t):
                pair, t, _, _ = place(j, t)
                dve.wait_ge(biased, pair * 2 * TILES + 2 * t + 2)
                if not (is_first(pair) and t < 2):
                    dve.wait_ge(exp_done, pair * TILES + t - 1)
                vec.tensor_tensor(neg_max[:, t % 2:t % 2 + 1], neg_max_h[:, t % 2, 0:1], neg_max_h[:, t % 2, 1:2],
                                  ALU.min).then_inc(max_done, 1)

            def evacuate(j, t, g):
                dve.wait_ge(transposed, j * 4 * TILES + 4 * t + g + 1)
                if t >= 1:
                    dve.wait_ge(pv_done, j * 4 * TILES + 4 * (t - 1) + g + 1)
                elif not is_first(j):
                    dve.wait_ge(pv_done, j * 4 * TILES)
                vec.tensor_copy(pT[:, g], tr_ps[g % 2][:]).then_inc(evac_dve, 1)

            def normalise(j, t):
                s = t % RING
                dve.wait_ge(exp_done, j * TILES + t + 1)
                vec.reciprocal(inv_sum[:, s:s + 1], row_sum[:, s:s + 1]).then_inc(inv_done, 1)
                dve.wait_ge(inv_done, j * TILES + t + 1)
                dve.wait_ge(pv_done, j * 4 * TILES + 4 * t + 4)
                if not (is_first(j) and t < RING):
                    dve.wait_ge(o_out[s], j * (TILES // RING) * 16 + t // RING * 16)
                vec.tensor_scalar(o_norm[:, s, :], o_ps[:, 0:D], inv_sum[:, s:s + 1], None,
                                  ALU.mult).then_inc(normed, 1)

            bias(0, 0, 0)
            bias(0, 0, 1)
            maximum(0, 0)
            bias(0, 1, 0)

            def body(j, last):
                for t in range(TILES):
                    if t + 1 < TILES or not last:
                        bias(j, t + 1, 1)
                        maximum(j, t + 1)
                    evacuate(j, t, 1)
                    if t >= 1:
                        normalise(j, t - 1)
                    evacuate(j, t, 2)
                    if t + 2 < TILES or not last:
                        bias(j, t + 2, 0)
                normalise(j, TILES - 1)

            body(0, False)
            with dve.Fori(1, NPAIR - 1) as j:
                body(j, False)
            body(NPAIR - 1, True)

            dve.wait_ge(fin_in, 48)
            chain(vec.tensor_scalar(sgn, fw_raw, 0.0, None, ALU.is_gt), fin_step)
            chain(vec.tensor_scalar(sgn_neg, fw_raw, 0.0, None, ALU.is_lt), fin_step)
            vec.tensor_tensor(sgn, sgn, sgn_neg, ALU.subtract).then_inc(sign_done, 1)
            norms = [0]

            def layernorm(dst, src):
                norms[0] += 1
                chain(vec.bn_stats(stats, src), fin_step)
                vec.bn_aggr(mean_var, stats).then_inc(var_done, 1)
                dve.wait_ge(std_done, norms[0])
                chain(vec.reciprocal(inv_std, std), fin_step)
                return vec.tensor_scalar(dst, src, mean_var[:, 0:1], inv_std, ALU.subtract, ALU.mult)

            for i in range(NT + 1):
                if i < NT:
                    dve.wait_ge(attn_done, i + 1)
                    chain(vec.tensor_tensor(x_res[:, i, :], o_ps[:, 0:P], x_res[:, i, :], ALU.add), fin_step)
                    layernorm(x1[:, i, :], x_res[:, i, :]).then_inc(x1_done, 1)
                if i >= 1:
                    dve.wait_ge(x1_done, i)
                    dve.wait_ge(ffn_done, i)
                    chain(vec.tensor_tensor(x_res[:, i - 1, :], sc_ps[:, (i - 1) % 2, 0:P], x1[:, i - 1, :], ALU.add),
                          fin_step)
                    layernorm(y_fin[:, i - 1, :], x_res[:, i - 1, :]).then_inc(y_done, 1)

        @block.scalar
        def _(act):
            sca = nc.scalar
            act.wait_ge(angles, 1)
            sca.activation(sin_q, ang, ACT.Sin).then_inc(sines, 1)
            sca.activation(half_s, ang, ACT.Sin, scale=0.5).then_inc(sines, 1)

            def project_out(pair, c):
                act.wait_ge(proj_done, pair * CHUNKS + c + 1)
                if c < 8:
                    x = c // 4
                    if c % 4 == 0 and not is_first(pair):
                        act.wait_ge(rope_step, (pair * 2 + x - 1) * ROPE_STEPS)
                    if c == 4 and is_first(pair):
                        act.wait_ge(tables, 1)
                    s0 = (c % 4) * 512
                    sca.activation(raw[x][:, s0:s0 + 512], pj_ps[:], ACT.Copy,
                                   scale=(-SCALE if x == 0 else 1.0)).then_inc(proj_out, 1)
                else:
                    n = (c - 8) * 4
                    both = pj_ps[:].rearrange("p (n h d) -> p n h d", n=4, h=2)
                    if c == 8 and not is_first(pair):
                        act.wait_ge(pv_done, (pair - 1) * 4 * TILES + 4 * NT)
                        act.wait_ge(v_moved, pair)
                    sca.activation(v_sb[0][:, n:n + 4, :], both[:, :, 0, :], ACT.Copy)
                    sca.activation(v_next[:, n:n + 4, :], both[:, :, 1, :], ACT.Copy).then_inc(proj_out, 1)

            act.wait_ge(params, 2)
            act.wait_ge(consts, 6)
            for b in range(2):
                sca.activation(bias_row[b], bias_row[b], ACT.Ln, scale=a_c[:, 0:1], bias=1.0).then_inc(logs, 1)
            for c in range(CHUNKS):
                project_out(0, c)

            def exponential(j, t):
                pair, t, _, _ = place(j, t)
                act.wait_ge(max_done, pair * TILES + t + 1)
                if not is_first(pair):
                    if isinstance(j, int) or t >= RING or t == 0:
                        act.wait_ge(inv_done, pair * TILES + t - RING + 1)
                    else:
                        act.wait_ge(inv_done, pair * TILES)
                sca.activation(prob[t % 2][:], prob[t % 2][:], ACT.Exp, bias=neg_max[:, t % 2:t % 2 + 1], scale=-1.0,
                               accum_out=row_sum[:, t % RING:t % RING + 1]).then_inc(exp_done, 1)

            def evacuate(j, t, g):
                act.wait_ge(transposed, j * 4 * TILES + 4 * t + g + 1)
                if t >= 1:
                    act.wait_ge(pv_done, j * 4 * TILES + 4 * (t - 1) + g + 1)
                elif not is_first(j):
                    act.wait_ge(pv_done, j * 4 * TILES)
                sca.activation(pT[:, g], tr_ps[g % 2][:], ACT.Copy).then_inc(evac_act, 1)

            exponential(0, 0)

            def body(j, last):
                for t in range(TILES):
                    evacuate(j, t, 0)
                    if t + 1 < TILES or not last:
                        exponential(j, t + 1)
                    if not last and t in CHUNK_TILE:
                        project_out(j + 1, CHUNK_TILE[t])
                    evacuate(j, t, 3)

            body(0, False)
            with act.Fori(1, NPAIR - 1) as j:
                body(j, False)
            body(NPAIR - 1, True)

            def o_evacuate(i):
                for g in range(2):
                    act.wait_ge(o_tr, 2 * i + g + 1)
                    if g == 0 and i >= 2:
                        act.wait_ge(attn_done, i - 1)
                    sca.activation(oT[:, i % 2, 4 * g:4 * g + 4, :], tr_ps[g][:], ACT.Copy).then_inc(oT_out, 1)

            roots = [0]

            def root():
                roots[0] += 1
                act.wait_ge(var_done, roots[0])
                sca.activation(std, mean_var[:, 1:2], ACT.Sqrt, bias=EPS).then_inc(std_done, 1)

            o_evacuate(0)
            for i in range(NT + 1):
                if i >= 1:
                    act.wait_ge(x1_tr, i)
                    if i >= 3:
                        act.wait_ge(ffn_done, i - 2)
                    sca.activation(x1T[:, (i - 1) % 2, :], pj_ps[:, 0:P], ACT.Copy).then_inc(x1T_out, 1)
                if i < NT:
                    root()
                if i + 1 < NT:
                    o_evacuate(i + 1)
                if i >= 1:
                    root()


def kernel(L0_attn_x, L0_attn_qkv_w, L0_attn_out_w, L0_attn_bias_p, L0_attn_bias_a, L0_attn_rope_freqs,
           L0_ffn_weight):
    import concourse.bacc as bacc
    from concourse.bass_utils import run_bass_kernel_spmd

    x = np.asarray(L0_attn_x)
    arrays = {
        "xT": np.ascontiguousarray(x[0].T),
        "x": np.ascontiguousarray(x),
        "wqkvT": np.ascontiguousarray(np.asarray(L0_attn_qkv_w).reshape(3, H * D, DM).transpose(2, 0, 1)),
        "owT": np.ascontiguousarray(np.asarray(L0_attn_out_w).reshape(DM, 8, P).transpose(2, 1, 0)),
        "bias_p": np.ascontiguousarray(np.asarray(L0_attn_bias_p).reshape(H, 1)),
        "bias_a": np.ascontiguousarray(np.asarray(L0_attn_bias_a).reshape(H, 1)),
        "freqs": np.ascontiguousarray(np.asarray(L0_attn_rope_freqs).reshape(D // 2, 1)),
        "ffnT": np.ascontiguousarray(np.asarray(L0_ffn_weight).T),
    }
    nc = bacc.Bacc("TRN2", target_bir_lowering=False, num_devices=1)
    args = [nc.dram_tensor(n, a.shape, mybir.dt.from_np(a.dtype), kind="ExternalInput").ap()
            for n, a in arrays.items()]
    out = nc.dram_tensor("out", (1, S, DM), F32, kind="ExternalOutput").ap()
    rows = nc.dram_tensor("rows", (H, ROW), F32, kind="Internal").ap()
    o_dram = nc.dram_tensor("o_dram", (S, H * D), F32, kind="Internal").ap()
    layer(nc, *args, out, rows, o_dram)
    return run_bass_kernel_spmd(nc, [arrays], core_ids=[0]).results[0]["out"]
```

```python
from contextlib import ExitStack

import numpy as np

import concourse.bass as bass
from concourse import mybir

F32 = mybir.dt.float32
F32R = mybir.dt.float32r
ALU = mybir.AluOpType
ACT = mybir.ActivationFunctionType

P = 128
S = 2048
DM = 128
H = 16
D = 64
NT = S // P
NPAIR = H // 2
TILES = 2 * NT
HALF = S // 2
TOE = S + S - P
ROW = 2 * S
SCALE = 1.0 / float(np.sqrt(D))
EPS = 1e-5
BIG = 3.0e38
RING = 4
TABLE_DMAS = 16

CHUNK_TILE = {1: 0, 2: 1, 3: 2, 4: 3, 5: 4, 6: 5, 7: 6, 8: 7, 18: 8, 19: 9, 20: 10, 21: 11}
CHUNKS = 12

PREP = 28
PREP_Q, PREP_K, PREP_KSPLIT, PREP_Q0, PREP_V0, PREP_Q1, PREP_V1 = 6, 12, 16, 20, 22, 26, 28

ROUND = 1.5 * 2.0 ** 23
ROUND_HI = 1.5 * 2.0 ** 34
INV_2PI = float(np.float32(1.0 / (2.0 * np.pi)))


def two_pi_parts():
    rest, parts = 2.0 * np.pi, []
    for _ in range(3):
        unit = 2.0 ** (np.floor(np.log2(rest)) - 10)
        parts.append(float(np.floor(rest / unit) * unit))
        rest -= parts[-1]
    return parts, float(np.float32(rest))


def layer(nc, xT, x, wqkvT, owT, bias_p, bias_a, freqs, ffnT, out, rows):
    with ExitStack() as ctx:
        def sb(name, shape, dt=F32):
            return ctx.enter_context(nc.sbuf_tensor(name, shape, dt))

        def psum(name, shape):
            return ctx.enter_context(nc.psum_tensor(name, shape, F32))

        def sem(name):
            return ctx.enter_context(nc.semaphore(name))

        xT_sb = sb("xT_sb", [P, S])
        w_sb = sb("w_sb", [P, 3, P])
        ow_sb = [sb(f"ow{h}", [P, DM]) for h in range(2)]
        rope_t = sb("rope_t", [P, 2, S])
        sin_t, cos_t = rope_t[:, 0], rope_t[:, 1]
        raw = [sb("raw_q", [P, S]), sb("raw_k", [P, S])]
        rot = sb("rot", [P, S])
        q_hi = [sb(f"q_hi{h}", [P, S], F32R) for h in range(2)]
        q_lo = [sb(f"q_lo{h}", [P, S], F32R) for h in range(2)]
        k_hl = [sb(f"k_hl{h}", [P, S], F32R) for h in range(2)]
        toe = [sb(f"toe{h}", [P, TOE]) for h in range(2)]
        v_hl = [sb(f"v_hl{h}", [P, NT, 2, D], F32R) for h in range(2)]
        v_stage = sb("v_stage", [P, NT, 2, D])
        prob = [sb(f"prob{b}", [P, S]) for b in range(2)]
        pT = [sb(f"pT{b}", [P, 4, 2, P], F32R) for b in range(5)]
        pT_stage = [sb(f"pT_stage{b}", [P, 4, P]) for b in range(2)]
        o_part = sb("o_part", [P, P])
        o_sum = [sb(f"o_sum{b}", [P, P]) for b in range(2)]
        y = sb("y", [P, NT, DM])
        ident = sb("ident", [P, P])
        neg_max_h = sb("neg_max_h", [P, 2, 2])
        neg_max = sb("neg_max", [P, 2])
        row_sum = sb("row_sum", [P, RING])
        inv_sum = sb("inv_sum", [P, RING])
        freq_c = sb("freq_c", [P, 1])
        offset = sb("offset", [P, 1])
        a_c = sb("a_c", [H, 1])
        p_c = sb("p_c", [H, 1])

        sc_ps = psum("sc_ps", [P, 4, 512])
        tr_ps = [psum(f"tr_ps{b}", [P, 4, P]) for b in range(2)]
        o_ps = psum("o_ps", [P, 512])
        pj_ps = psum("pj_ps", [P, 512])

        W = S // 4
        ang, turns, t_hi, t_lo = (prob[0][:, n * W:n * W + W] for n in range(4))
        nsin_q, cos_even, sin_q, cos_odd = (prob[1][:, n * W:n * W + W] for n in range(4))
        col = nsin_q
        half_s = rot[:, 0:W]
        rot_k0 = prob[0]
        bias_row = [toe[b][0:H, 0:S] for b in range(2)]

        x1 = raw[0][:, :].rearrange("p (t d) -> p t d", t=NT)
        y_fin = raw[1][:, :].rearrange("p (t d) -> p t d", t=NT)
        fw_raw, sgn, sgn_neg = (cos_t[:, n * P:n * P + P] for n in range(3))
        x1T = cos_t[:, 512:512 + 4 * P].rearrange("p (b q) -> p b q", b=4)
        stats = cos_t[:, 1024:1024 + 8 * NT].rearrange("p (t n) -> p t n", t=NT)
        mean_var = cos_t[:, 1280:1280 + 2 * NT].rearrange("p (t n) -> p t n", t=NT)
        std = cos_t[:, 1344:1344 + NT]
        inv_std = cos_t[:, 1408:1408 + NT]

        x_in = sem("x_in")
        y_in = sem("y_in")
        w_in = sem("w_in")
        ow_in = [sem(f"ow_in{h}") for h in range(2)]
        freq_in = sem("freq_in")
        small_in = sem("small_in")
        consts = sem("consts")
        dve_step = sem("dve_step")
        angles = sem("angles")
        params = sem("params")
        sines = sem("sines")
        tables = sem("tables")
        tab_in = sem("tab_in")
        logs = sem("logs")
        rows_done = sem("rows_done")
        rows_out = sem("rows_out")
        toe_in = [sem(f"toe_in{h}") for h in range(2)]
        q_in = [sem(f"q_in{h}") for h in range(2)]
        k_in = [sem(f"k_in{h}") for h in range(2)]
        rot_in = [sem("rot_in_q"), sem("rot_in_k")]
        prep = sem("prep")
        cos_scaled = sem("cos_scaled")
        sin_scaled = sem("sin_scaled")
        proj_done = sem("proj_done")
        proj_out = sem("proj_out")
        scored = sem("scored")
        biased = sem("biased")
        max_done = sem("max_done")
        exp_done = sem("exp_done")
        transposed = sem("transposed")
        staged = sem("staged")
        hi_done = sem("hi_done")
        lo_done = sem("lo_done")
        split_done = sem("split_done")
        pv_done = sem("pv_done")
        o_copied = sem("o_copied")
        o_added = sem("o_added")
        out_done = sem("out_done")
        inv_done = sem("inv_done")
        y_added = sem("y_added")
        fw_in = sem("fw_in")
        sign_done = sem("sign_done")
        fin_step = sem("fin_step")
        stats_done = sem("stats_done")
        var_done = sem("var_done")
        std_done = sem("std_done")
        x1_done = sem("x1_done")
        x1_tr = sem("x1_tr")
        x1T_out = sem("x1T_out")
        ffn_done = sem("ffn_done")
        y2_added = sem("y2_added")
        y_done = sem("y_done")
        y_out = sem("y_out")

        def is_first(pair):
            return isinstance(pair, int) and pair == 0

        def exists(j, t):
            return not isinstance(j, int) or 0 <= j * TILES + t < NPAIR * TILES

        def ready(eng, value):
            return value if isinstance(value, int) else eng.to_reg(value)

        def project_bank(pair, c):
            return sc_ps[:, c % 4] if is_first(pair) else pj_ps[:]

        def pT_slot(t, g):
            return pT[g] if g else pT[4 * (t % 2)]

        block = ctx.enter_context(nc.Block())

        @block.sync
        def _(sp):
            sp.dma_start(freq_c[:], freqs[:, :]).then_inc(freq_in, 16)
            sp.dma_start(w_sb[:], wqkvT[:, :, 0:P]).then_inc(w_in, 16)
            sp.dma_start(xT_sb[:], xT[:, :]).then_inc(x_in, 16)
            sp.dma_start(a_c[:], bias_a[:, :]).then_inc(small_in, 16)
            sp.dma_start(p_c[:], bias_p[:, :]).then_inc(small_in, 16)

            def rotate(pair, x):
                n_out = ready(sp, pair * CHUNKS + 4 * x + 4)
                n_before = ready(sp, pair * PREP + PREP_Q if x else pair * 32)
                sp.wait_ge(proj_out, n_out)
                if x == 1 and is_first(pair):
                    sp.wait_ge(sines, 2)
                elif x == 1:
                    sp.wait_ge(prep, n_before)
                elif not is_first(pair):
                    sp.wait_ge(k_in[1], n_before)
                dst = rot_k0 if x == 1 and is_first(pair) else rot
                for a in range(4):
                    b = a ^ 1
                    sp.dma_start(dst[32 * a:32 * a + 32], raw[x][32 * b:32 * b + 32]).then_inc(rot_in[x], 16)

            def stack_q(pair, h):
                n_rope = ready(sp, pair * PREP + PREP_Q)
                n_biased = ready(sp, (pair - 1) * 2 * TILES + 2 * NT * (h + 1))
                sp.wait_ge(prep, n_rope)
                if not is_first(pair):
                    sp.wait_ge(biased, n_biased)
                for half in (slice(0, D), slice(D, P)):
                    sp.dma_start(q_lo[h][half].bitcast(F32), raw[0][D * h:D * h + D]).then_inc(q_in[h], 16)

            def stack_k(pair, h):
                n_hi = ready(sp, pair * PREP + PREP_KSPLIT - 2)
                n_lo = ready(sp, pair * PREP + PREP_KSPLIT)
                n_biased = ready(sp, (pair - 1) * 2 * TILES + 2 * NT * (h + 1))
                sp.wait_ge(prep, n_hi)
                if not is_first(pair):
                    sp.wait_ge(biased, n_biased)
                sp.dma_start(k_hl[h][0:D].bitcast(F32), rot[D * h:D * h + D]).then_inc(k_in[h], 16)
                sp.wait_ge(prep, n_lo)
                sp.dma_start(k_hl[h][D:P].bitcast(F32), raw[1][D * h:D * h + D]).then_inc(k_in[h], 16)

            def toeplitz(pair, h):
                n = 2 * pair + h
                row = rows[n:n + 1, :] if isinstance(pair, int) else rows[bass.ds(n, 1), :]
                n_biased = ready(sp, (pair - 1) * 2 * TILES + 2 * NT * (h + 1))
                sp.wait_ge(rows_out, 32)
                if not is_first(pair):
                    sp.wait_ge(biased, n_biased)
                sp.dma_start(toe[h][:], bass.AP(tensor=row.tensor, offset=row.offset,
                                                ap=[[1, P], [1, TOE]])).then_inc(toe_in[h], 16)

            def load_ow(pair, h):
                n = 2 * pair + h
                src = owT[n:n + 1] if isinstance(pair, int) else owT[bass.ds(n, 1)]
                n_out = ready(sp, (pair - 1) * TILES + NT * (h + 1))
                sp.wait_ge(x_in, 16)
                if not is_first(pair):
                    sp.wait_ge(out_done, n_out)
                sp.dma_start(ow_sb[h][:], src.rearrange("a p d -> (a p) d")).then_inc(ow_in[h], 16)

            sp.wait_ge(tables, 3)
            for a in range(4):
                for b in range(4):
                    n = 2 * W * (a % 2)
                    sp.dma_start(rope_t[32 * a:32 * a + 32, :, W * b:W * b + W],
                                 prob[1][32 * b:32 * b + 32, n:n + 2 * W].rearrange("p (n w) -> p n w", n=2)
                                 ).then_inc(tab_in, 16)
            rotate(0, 0)
            rotate(0, 1)
            sp.wait_ge(rows_done, 2)
            for b in range(2):
                sp.dma_start(rows[:, b * S:b * S + S], bias_row[b]).then_inc(rows_out, 16)
            toeplitz(0, 0)
            stack_q(0, 0)
            stack_k(0, 0)
            stack_q(0, 1)
            stack_k(0, 1)
            toeplitz(0, 1)
            sp.dma_start(y[:], x[0].rearrange("(t p) d -> p t d", p=P)).then_inc(y_in, 16)
            load_ow(0, 0)

            def body(j, last):
                if last:
                    load_ow(j, 1)
                    sp.wait_ge(prep, NPAIR * PREP - 6)
                    sp.dma_start(fw_raw, ffnT[:, :]).then_inc(fw_in, 16)
                    return
                n_proj = ready(sp, j * CHUNKS + CHUNKS)
                sp.wait_ge(x_in, 16)
                sp.wait_ge(proj_done, n_proj)
                sp.dma_start(w_sb[:], wqkvT[:, :, bass.ds(j * P + P, P)]).then_inc(w_in, 16)
                load_ow(j, 1)
                rotate(j + 1, 0)
                rotate(j + 1, 1)
                stack_q(j + 1, 0)
                toeplitz(j + 1, 0)
                load_ow(j + 1, 0)
                stack_k(j + 1, 0)
                stack_q(j + 1, 1)
                stack_k(j + 1, 1)
                toeplitz(j + 1, 1)

            body(0, False)
            with sp.Fori(1, NPAIR - 1) as j:
                body(j, False)
            body(NPAIR - 1, True)

            for g in range(NT // 4):
                sp.wait_ge(y_done, 4 * g + 4)
                sp.dma_start(out[0, 4 * g * P:4 * (g + 1) * P].rearrange("(t p) d -> p t d", p=P),
                             y_fin[:, 4 * g:4 * g + 4]).then_inc(y_out, 16)
            sp.wait_ge(y_out, NT // 4 * 16)

        def cols(n):
            return slice(n * HALF, n * HALF + HALF)

        @block.gpsimd
        def _(pool):
            made = [0]

            def make(ins):
                made[0] += 1
                ins.then_inc(consts, 1)
                pool.wait_ge(consts, made[0])

            exact = dict(channel_multiplier=0, allow_small_or_imprecise_dtypes=True)
            make(nc.gpsimd.iota(col, pattern=[[1, W]], base=0, **exact))
            for b in range(4):
                make(nc.gpsimd.iota(offset[32 * b:32 * b + 32], pattern=[[1, 1]], base=W * b, **exact))
            make(nc.gpsimd.iota(bias_row[0], pattern=[[-1, S]], base=S - 1, **exact))
            make(nc.gpsimd.iota(bias_row[1], pattern=[[1, S]], base=1, **exact))
            make(nc.gpsimd.memset(ident[:], 0.0))
            make(nc.gpsimd.affine_select(out=ident[:], in_=ident[:], compare_op=ALU.not_equal, fill=1.0, base=0,
                                         pattern=[[-1, P]], channel_multiplier=1))
            pool.wait_ge(tab_in, TABLE_DMAS * 16)
            for x, turned in enumerate((rot, rot_k0)):
                pool.wait_ge(rot_in[x], 64)
                nc.gpsimd.tensor_tensor(turned[:], turned[:], sin_t, ALU.mult).then_inc(sin_scaled, 1)

            def rope(pair, x, n):
                c = cols(n % 2)
                if n == 0:
                    n_out = ready(pool, pair * CHUNKS + 4 * x + 4)
                    n_rot = ready(pool, pair * 64 + 64)
                    pool.wait_ge(proj_out, n_out)
                    pool.wait_ge(rot_in[x], n_rot)
                if n < 2:
                    return nc.gpsimd.tensor_tensor(raw[x][:, c], raw[x][:, c], cos_t[:, c], ALU.mult)
                if n < 4:
                    return nc.gpsimd.tensor_tensor(rot[:, c], rot[:, c], sin_t[:, c], ALU.mult)
                pool.wait_ge(prep, pair * PREP + (PREP_K if x else PREP_Q) - 6 + n)
                return nc.gpsimd.tensor_tensor(raw[x][:, c], raw[x][:, c], rot[:, c], ALU.add)

            def split_k(pair, n):
                c = cols(n % 2)
                n_before = ready(pool, pair * PREP + PREP_K + n)
                pool.wait_ge(tab_in, TABLE_DMAS * 16)
                pool.wait_ge(prep, n_before)
                if n < 2:
                    return nc.gpsimd.tensor_copy(rot[:, c].bitcast(F32R), raw[1][:, c])
                return nc.gpsimd.tensor_tensor(raw[1][:, c], raw[1][:, c], rot[:, c], ALU.subtract)

            def split_q(pair, h, n):
                c = cols(n % 2)
                n_before = ready(pool, pair * PREP + (PREP_Q1 if h else PREP_Q0) - 4 + n)
                n_in = ready(pool, pair * 32 + 32)
                pool.wait_ge(tab_in, TABLE_DMAS * 16)
                if n == 0:
                    pool.wait_ge(q_in[h], n_in)
                pool.wait_ge(prep, n_before)
                if n < 2:
                    return nc.gpsimd.tensor_copy(q_hi[h][:, c], q_lo[h][:, c].bitcast(F32))
                return nc.gpsimd.tensor_tensor(q_lo[h][:, c], q_lo[h][:, c].bitcast(F32), q_hi[h][:, c].bitcast(F32),
                                               ALU.subtract)

            def split_v(pair, h, n):
                n_out = ready(pool, pair * CHUNKS + CHUNKS)
                n_pv = ready(pool, (pair - 1) * 4 * TILES + 4 * NT * (h + 1))
                n_before = ready(pool, pair * PREP + (PREP_V1 if h else PREP_V0) - 2 + n)
                pool.wait_ge(tab_in, TABLE_DMAS * 16)
                if n == 0:
                    pool.wait_ge(proj_out, n_out)
                    if not is_first(pair):
                        pool.wait_ge(pv_done, n_pv)
                pool.wait_ge(prep, n_before)
                if n == 0:
                    return nc.gpsimd.tensor_copy(v_hl[h][:, :, 0, :], v_stage[:, :, h, :])
                return nc.gpsimd.tensor_tensor(v_hl[h][:, :, 1, :], v_stage[:, :, h, :],
                                               v_hl[h][:, :, 0, :].bitcast(F32), ALU.subtract)

            def split_p(j, t):
                c = j * TILES + t
                slot = pT_slot(t, 0)
                pool.wait_ge(staged, c + 1)
                pool.wait_ge(hi_done, 4 * c + 4)
                nc.gpsimd.tensor_tensor(slot[:, :, 1, :], pT_stage[t % 2][:], slot[:, :, 0, :].bitcast(F32),
                                        ALU.subtract).then_inc(split_done, 1)

            def body(j, last):
                for t in range(TILES):
                    split_p(j, t)
                    if t < 4:
                        split_q(j, 1, t).then_inc(prep, 1)
                    elif t < 6:
                        split_v(j, 1, t - 4).then_inc(prep, 1)
                    elif last:
                        continue
                    elif 7 <= t < 13:
                        rope(j + 1, 0, t - 7).then_inc(prep, 1)
                    elif 15 <= t < 21:
                        rope(j + 1, 1, t - 15).then_inc(prep, 1)
                    elif 21 <= t < 25:
                        split_k(j + 1, t - 21).then_inc(prep, 1)
                    elif 25 <= t < 29:
                        split_q(j + 1, 0, t - 25).then_inc(prep, 1)
                    elif 29 <= t < 31:
                        split_v(j + 1, 0, t - 29).then_inc(prep, 1)

            body(0, False)
            with pool.Fori(1, NPAIR - 1) as j:
                body(j, False)
            body(NPAIR - 1, True)

        @block.tensor
        def _(pe):
            def project(pair, c, after):
                if c == 0:
                    pe.wait_ge(w_in, pair * 16 + 16)
                ps = project_bank(pair, c)
                if not is_first(pair):
                    pe.wait_ge(proj_out, pair * CHUNKS + c)
                elif c >= 4:
                    pe.wait_ge(proj_out, c - 3)
                if after is not None:
                    pe.wait_ge(y_added, after)
                if c < 8:
                    s0 = (c % 4) * 512
                    mm = nc.tensor.matmul(ps, w_sb[:, c // 4, :], xT_sb[:, s0:s0 + 512], start=True, stop=True)
                else:
                    for n in range(4):
                        s0 = ((c - 8) * 4 + n) * P
                        mm = nc.tensor.matmul(ps[:, n * P:n * P + P], xT_sb[:, s0:s0 + P], w_sb[:, 2, :],
                                              start=True, stop=True)
                mm.then_inc(proj_done, 1)

            def score(j, t, half):
                if not exists(j, t):
                    return
                c, pair = j * TILES + t, j + t // TILES
                h, i = t % TILES // NT, t % NT
                if i == 0 and half == 0:
                    pe.wait_ge(prep, pair * PREP + (PREP_Q1 if h else PREP_Q0))
                    pe.wait_ge(k_in[h], pair * 32 + 32)
                if exists(j, t - 1):
                    pe.wait_ge(biased, 2 * c + half - 1)
                for n, q in enumerate((q_hi[h], q_lo[h])):
                    for b in (2 * half, 2 * half + 1):
                        mm = nc.tensor.matmul(sc_ps[:, b], q[:, i * P:i * P + P], k_hl[h][:, b * 512:b * 512 + 512],
                                              start=(n == 0), stop=(n == 1))
                mm.then_inc(scored, 1)

            def transpose(j, t, g):
                c = j * TILES + t
                if g == 0:
                    pe.wait_ge(exp_done, c + 1)
                if g == 2:
                    pe.wait_ge(staged, c + 1)
                elif g == 3:
                    pe.wait_ge(lo_done, 3 * c + 1)
                elif exists(j, t - 1):
                    pe.wait_ge(lo_done, 3 * c - 1 + g)
                for n in range(4):
                    k0 = (4 * g + n) * P
                    mm = nc.tensor.transpose(tr_ps[g % 2][:, n, :], prob[t % 2][:, k0:k0 + P], ident[:])
                mm.then_inc(transposed, 1)

            def values(j, t, g):
                if not exists(j, t):
                    return
                c, pair, h = j * TILES + t, j + t // TILES, t % TILES // NT
                if g:
                    pe.wait_ge(lo_done, 3 * c + g)
                else:
                    pe.wait_ge(split_done, c + 1)
                if t % NT == 0 and g == 1:
                    pe.wait_ge(prep, pair * PREP + (PREP_V1 if h else PREP_V0))
                if g == 1 and exists(j, t - 1):
                    pe.wait_ge(o_added, c)
                slot = pT_slot(t, g)
                for n in range(4):
                    mm = nc.tensor.matmul(o_ps[:, 0:2 * P], v_hl[h][:, 4 * g + n, :, :].rearrange("p a d -> p (a d)"),
                                          slot[:, n, :, :].rearrange("p a q -> p (a q)"),
                                          start=(g == 1 and n == 0), stop=(g == 0 and n == 3))
                mm.then_inc(pv_done, 1)

            def project_out(j, t, chunk):
                if not exists(j, t):
                    return
                c, pair, h = j * TILES + t, j + t // TILES, t % TILES // NT
                if t % NT == 0:
                    pe.wait_ge(ow_in[h], pair * 16 + 16)
                pe.wait_ge(o_added, c + 1)
                pe.wait_ge(proj_out, chunk)
                if exists(j, t - 1):
                    pe.wait_ge(y_added, c)
                nc.tensor.matmul(pj_ps[:, 0:DM], o_sum[t % 2][:], ow_sb[h][:], start=True, stop=True).then_inc(out_done, 1)

            pe.wait_ge(x_in, 16)
            for c in range(CHUNKS):
                project(0, c, None)
            pe.wait_ge(consts, 9)
            pe.wait_ge(proj_out, CHUNKS)
            for t in range(2):
                for half in range(2):
                    score(0, t, half)

            def body(j, last):
                chunks = 0
                for t in range(TILES):
                    transpose(j, t, 0)
                    project_out(j, t - 2, j * CHUNKS + CHUNKS + chunks)
                    values(j, t - 1, 1)
                    values(j, t - 1, 2)
                    transpose(j, t, 1)
                    transpose(j, t, 2)
                    values(j, t - 1, 3)
                    score(j, t + 2, 0)
                    if not last and t in CHUNK_TILE:
                        project(j + 1, CHUNK_TILE[t], j * TILES + t - 1 if exists(j, t - 2) else None)
                        chunks += 1
                    values(j, t - 1, 0)
                    transpose(j, t, 3)
                    score(j, t + 2, 1)

            body(0, False)
            with pe.Fori(1, NPAIR - 1) as j:
                body(j, False)
            body(NPAIR - 1, True)
            end = NPAIR * TILES
            project_out(0, end - 2, NPAIR * CHUNKS)
            for g in (1, 2, 3, 0):
                values(0, end - 1, g)
            project_out(0, end - 1, NPAIR * CHUNKS)

            pe.wait_ge(sign_done, 1)
            for i in range(NT + 1):
                if i < NT:
                    pe.wait_ge(x1_done, i + 1)
                    if i == 0:
                        pe.wait_ge(y_added, end)
                    if i >= 2:
                        pe.wait_ge(x1T_out, i - 1)
                    nc.tensor.transpose((pj_ps, o_ps)[i % 2][:, 0:P], x1[:, i, :], ident[:]).then_inc(x1_tr, 1)
                if i >= 1:
                    pe.wait_ge(x1T_out, i)
                    if i >= 5:
                        pe.wait_ge(y2_added, i - 4)
                    nc.tensor.matmul(sc_ps[:, (i - 1) % 4, 0:P], x1T[:, (i - 1) % 4, :], sgn,
                                     start=True, stop=True).then_inc(ffn_done, 1)

        @block.vector
        def _(dve):
            vec = nc.vector
            steps = {dve_step: 0, fin_step: 0}

            def chain(ins, on):
                steps[on] += 1
                ins.then_inc(on, 1)
                dve.wait_ge(on, steps[on])

            parts, rest = two_pi_parts()
            dve.wait_ge(consts, 5)
            dve.wait_ge(freq_in, 16)
            chain(vec.tensor_scalar(ang, col, offset[:, 0:1], freq_c[:, 0:1], ALU.add, ALU.mult), dve_step)
            chain(vec.tensor_scalar(t_hi, ang, INV_2PI, ROUND, ALU.mult, ALU.add), dve_step)
            chain(vec.tensor_scalar(turns, t_hi, ROUND, None, ALU.subtract), dve_step)
            chain(vec.tensor_scalar(t_hi, turns, ROUND_HI, ROUND_HI, ALU.add, ALU.subtract), dve_step)
            chain(vec.tensor_tensor(t_lo, turns, t_hi, ALU.subtract), dve_step)
            for part in parts:
                for n in (t_hi, t_lo):
                    chain(vec.scalar_tensor_tensor(out=ang, in0=n, scalar=-part, in1=ang, op0=ALU.mult, op1=ALU.add),
                          dve_step)
            chain(vec.scalar_tensor_tensor(out=ang, in0=turns, scalar=-rest, in1=ang, op0=ALU.mult, op1=ALU.add),
                  dve_step)
            vec.tensor_scalar(ang, ang, 3.1415925, -3.1415925, ALU.min, ALU.max).then_inc(angles, 1)
            dve.wait_ge(small_in, 32)
            vec.tensor_scalar(a_c[:], a_c[:], 0.01, None, ALU.max).then_inc(params, 1)
            vec.tensor_scalar(p_c[:], p_c[:], 0.01, None, ALU.max).then_inc(params, 1)
            dve.wait_ge(sines, 2)
            chain(vec.tensor_tensor(half_s, half_s, half_s, ALU.mult), dve_step)
            for cos_q in (cos_even, cos_odd):
                vec.tensor_scalar(cos_q, half_s, -2.0, 1.0, ALU.mult, ALU.add).then_inc(tables, 1)
            vec.tensor_scalar(nsin_q, sin_q, -1.0, None, ALU.mult).then_inc(tables, 1)
            dve.wait_ge(params, 2)
            for b in range(2):
                dve.wait_ge(logs, b + 1)
                vec.tensor_scalar(bias_row[b], bias_row[b], p_c[:, 0:1], None, ALU.mult).then_inc(rows_done, 1)

            def prepare(ins, n, before):
                ins.then_inc(prep, n)
                dve.wait_ge(prep, before + n)

            dve.wait_ge(tab_in, TABLE_DMAS * 16)
            for x in range(2):
                dve.wait_ge(proj_out, 4 * x + 4)
                dve.wait_ge(rot_in[x], 64)
                vec.tensor_tensor(raw[x][:], raw[x][:], cos_t, ALU.mult).then_inc(cos_scaled, 1)
            for x, base, turned in ((0, 0, rot), (1, PREP_Q, rot_k0)):
                dve.wait_ge(cos_scaled, x + 1)
                dve.wait_ge(sin_scaled, x + 1)
                prepare(vec.tensor_tensor(raw[x][:], raw[x][:], turned[:], ALU.add), 6, base)
            prepare(vec.tensor_copy(rot[:].bitcast(F32R), raw[1][:]), 2, PREP_K)
            prepare(vec.tensor_tensor(raw[1][:], raw[1][:], rot[:], ALU.subtract), 2, PREP_K + 2)
            dve.wait_ge(q_in[0], 32)
            prepare(vec.tensor_copy(q_hi[0][:], q_lo[0][:].bitcast(F32)), 2, PREP_KSPLIT)
            prepare(vec.tensor_tensor(q_lo[0][:], q_lo[0][:].bitcast(F32), q_hi[0][:].bitcast(F32), ALU.subtract),
                    2, PREP_KSPLIT + 2)

            def bias(j, t, half):
                if not exists(j, t):
                    return
                c, pair = j * TILES + t, j + t // TILES
                h, i = t % TILES // NT, t % NT
                n_scored = ready(dve, 2 * c + half + 1)
                n_toe = ready(dve, pair * 16 + 16) if i == 0 and half == 0 else None
                n_transposed = ready(dve, 4 * c - 6 + 2 * half)
                dve.wait_ge(tab_in, TABLE_DMAS * 16)
                if i == 0 and half == 0:
                    dve.wait_ge(toe_in[h], n_toe)
                dve.wait_ge(scored, n_scored)
                if exists(j, t - 2):
                    dve.wait_ge(transposed, n_transposed)
                c0 = P * i + S - HALF * (half + 1)
                vec.tensor_tensor_reduce(prob[t % 2][:, HALF * half:HALF * half + HALF],
                                         sc_ps[:, 2 * half:2 * half + 2].rearrange("p a b -> p (a b)"),
                                         toe[h][:, c0:c0 + HALF][:, ::-1], 1.0, BIG, ALU.add, ALU.min,
                                         neg_max_h[:, t % 2, half:half + 1]).then_inc(biased, 1)

            def maximum(j, t):
                if not exists(j, t):
                    return
                c = j * TILES + t
                dve.wait_ge(biased, 2 * c + 2)
                if exists(j, t - 2):
                    dve.wait_ge(exp_done, c - 1)
                vec.tensor_tensor(neg_max[:, t % 2:t % 2 + 1], neg_max_h[:, t % 2, 0:1], neg_max_h[:, t % 2, 1:2],
                                  ALU.min).then_inc(max_done, 1)

            def split_lo(j, t, g):
                c = j * TILES + t
                slot = pT_slot(t, g)
                dve.wait_ge(hi_done, 4 * c + g)
                vec.tensor_tensor(slot[:, :, 1, :], tr_ps[g % 2][:], slot[:, :, 0, :].bitcast(F32),
                                  ALU.subtract).then_inc(lo_done, 1)

            def add_output(j, t):
                if not exists(j, t):
                    return
                c = j * TILES + t
                dve.wait_ge(o_copied, c + 1)
                if exists(j, t - 2):
                    dve.wait_ge(out_done, c - 1)
                vec.tensor_tensor(o_sum[t % 2][:], o_ps[:, P:2 * P], o_part[:], ALU.add).then_inc(o_added, 1)

            def invert(j, t):
                c = j * TILES + t
                s = t % RING
                dve.wait_ge(exp_done, c + 1)
                if exists(j, t - RING):
                    dve.wait_ge(y_added, c - RING + 1)
                vec.reciprocal(inv_sum[:, s:s + 1], row_sum[:, s:s + 1]).then_inc(inv_done, 1)

            def residual(j, t):
                if not exists(j, t):
                    return
                c, i, s = j * TILES + t, t % NT, t % RING
                if is_first(j) and t == 0:
                    dve.wait_ge(y_in, 16)
                dve.wait_ge(inv_done, c + 1)
                dve.wait_ge(out_done, c + 1)
                vec.scalar_tensor_tensor(out=y[:, i, :], in0=pj_ps[:, 0:DM], scalar=inv_sum[:, s:s + 1],
                                         in1=y[:, i, :], op0=ALU.mult, op1=ALU.add).then_inc(y_added, 1)

            bias(0, 0, 0)
            bias(0, 0, 1)
            maximum(0, 0)
            bias(0, 1, 0)
            dve.wait_ge(proj_out, CHUNKS)
            prepare(vec.tensor_copy(v_hl[0][:, :, 0, :], v_stage[:, :, 0, :]), 1, PREP_Q0)
            prepare(vec.tensor_tensor(v_hl[0][:, :, 1, :], v_stage[:, :, 0, :], v_hl[0][:, :, 0, :].bitcast(F32),
                                      ALU.subtract), 1, PREP_Q0 + 1)

            residuals_before = (NPAIR - 1) * TILES

            def sign_weights():
                dve.wait_ge(fw_in, 16)
                chain(vec.tensor_scalar(sgn, fw_raw, 0.0, None, ALU.is_gt), fin_step)
                chain(vec.tensor_scalar(sgn_neg, fw_raw, 0.0, None, ALU.is_lt), fin_step)
                vec.tensor_tensor(sgn, sgn, sgn_neg, ALU.subtract).then_inc(sign_done, 1)

            def statistics(i):
                vec.bn_stats(stats[:, i, 0:6], y[:, i, :]).then_inc(stats_done, 1)

            def aggregate(i, before=0):
                dve.wait_ge(stats_done, before + i + 1)
                vec.bn_aggr(mean_var[:, i, :], stats[:, i, 0:6]).then_inc(var_done, 1)

            def body(j, last):
                for t in range(TILES):
                    bias(j, t + 1, 1)
                    residual(j, t - 2)
                    maximum(j, t + 1)
                    split_lo(j, t, 1)
                    split_lo(j, t, 2)
                    bias(j, t + 2, 0)
                    add_output(j, t - 1)
                    split_lo(j, t, 3)
                    invert(j, t)
                    if last and t == NT:
                        sign_weights()
                    if last and t >= NT + 3:
                        dve.wait_ge(y_added, residuals_before + t - 2)
                        statistics(t - NT - 3)
                    if last and t >= NT + 4:
                        aggregate(t - NT - 4)

            body(0, False)
            with dve.Fori(1, NPAIR - 1) as j:
                body(j, False)
            body(NPAIR - 1, True)
            end = NPAIR * TILES
            residual(0, end - 2)
            add_output(0, end - 1)

            residual(0, end - 1)
            dve.wait_ge(y_added, end)
            for i in range(NT - 3, NT):
                statistics(i)
            for i in range(NT - 4, NT):
                aggregate(i)
            dve.wait_ge(std_done, 1)
            chain(vec.reciprocal(inv_std, std), fin_step)
            for i in range(NT):
                vec.tensor_scalar(x1[:, i, :], y[:, i, :], mean_var[:, i, 0:1], inv_std[:, i:i + 1],
                                  ALU.subtract, ALU.mult).then_inc(x1_done, 1)
            dve.wait_ge(x1_done, NT)
            for i in range(NT + 2):
                if i < NT:
                    dve.wait_ge(ffn_done, i + 1)
                    vec.tensor_tensor(y[:, i, :], sc_ps[:, i % 4, 0:P], x1[:, i, :], ALU.add).then_inc(y2_added, 1)
                if 1 <= i <= NT:
                    dve.wait_ge(y2_added, i)
                    statistics(i - 1)
                if i >= 2:
                    aggregate(i - 2, NT)
            dve.wait_ge(std_done, 2)
            chain(vec.reciprocal(inv_std, std), fin_step)
            for i in range(NT):
                vec.tensor_scalar(y_fin[:, i, :], y[:, i, :], mean_var[:, i, 0:1], inv_std[:, i:i + 1],
                                  ALU.subtract, ALU.mult).then_inc(y_done, 1)

        @block.scalar
        def _(act):
            sca = nc.scalar
            act.wait_ge(angles, 1)
            sca.activation(sin_q, ang, ACT.Sin).then_inc(sines, 1)
            sca.activation(half_s, ang, ACT.Sin, scale=0.5).then_inc(sines, 1)

            def project_in(pair, c):
                ps = project_bank(pair, c)
                act.wait_ge(proj_done, pair * CHUNKS + c + 1)
                if c < 8:
                    x = c // 4
                    if c % 4 == 0 and not is_first(pair):
                        act.wait_ge((q_in, k_in)[x][1], pair * 32)
                    s0 = (c % 4) * 512
                    sca.activation(raw[x][:, s0:s0 + 512], ps, ACT.Copy,
                                   scale=(-SCALE if x == 0 else 1.0)).then_inc(proj_out, 1)
                else:
                    n = (c - 8) * 4
                    if c == 8 and not is_first(pair):
                        act.wait_ge(prep, pair * PREP)
                    sca.activation(v_stage[:, n:n + 4, :, :].rearrange("p n h d -> p (n h d)"), ps,
                                   ACT.Copy).then_inc(proj_out, 1)

            for c in range(CHUNKS):
                project_in(0, c)
            act.wait_ge(params, 2)
            act.wait_ge(consts, 7)
            for b in range(2):
                sca.activation(bias_row[b], bias_row[b], ACT.Ln, scale=a_c[:, 0:1], bias=1.0).then_inc(logs, 1)

            def exponential(j, t):
                if not exists(j, t):
                    return
                c = j * TILES + t
                act.wait_ge(max_done, c + 1)
                if exists(j, t - RING):
                    act.wait_ge(inv_done, c - RING + 1)
                sca.activation(prob[t % 2][:], prob[t % 2][:], ACT.Exp, bias=neg_max[:, t % 2:t % 2 + 1], scale=-1.0,
                               accum_out=row_sum[:, t % RING:t % RING + 1]).then_inc(exp_done, 1)

            def stage(j, t):
                c = j * TILES + t
                act.wait_ge(transposed, 4 * c + 1)
                if exists(j, t - 2):
                    act.wait_ge(split_done, c - 1)
                sca.activation(pT_stage[t % 2][:], tr_ps[0][:], ACT.Copy).then_inc(staged, 1)

            def split_hi(j, t, g):
                c = j * TILES + t
                if exists(j, t - 1):
                    act.wait_ge(pv_done, 4 * c - 4 + g)
                act.wait_ge(transposed, 4 * c + g + 1)
                sca.activation(pT_slot(t, g)[:, :, 0, :], tr_ps[g % 2][:], ACT.Copy).then_inc(hi_done, 1)

            def split_hi_stage(j, t):
                c = j * TILES + t
                act.wait_ge(staged, c + 1)
                if exists(j, t - 2):
                    act.wait_ge(pv_done, 4 * c - 4)
                sca.activation(pT_slot(t, 0)[:, :, 0, :], pT_stage[t % 2][:], ACT.Copy).then_inc(hi_done, 1)

            def copy_output(j, t):
                if not exists(j, t):
                    return
                c = j * TILES + t
                act.wait_ge(pv_done, 4 * c + 4)
                if exists(j, t - 1):
                    act.wait_ge(o_added, c)
                sca.activation(o_part[:], o_ps[:, 0:P], ACT.Copy).then_inc(o_copied, 1)

            exponential(0, 0)

            def body(j, last):
                for t in range(TILES):
                    stage(j, t)
                    split_hi(j, t, 1)
                    split_hi(j, t, 2)
                    exponential(j, t + 1)
                    copy_output(j, t - 1)
                    if not last and t in CHUNK_TILE:
                        project_in(j + 1, CHUNK_TILE[t])
                    split_hi(j, t, 3)
                    split_hi_stage(j, t)

            body(0, False)
            with act.Fori(1, NPAIR - 1) as j:
                body(j, False)
            body(NPAIR - 1, True)
            copy_output(0, NPAIR * TILES - 1)

            act.wait_ge(var_done, NT)
            sca.activation(std, mean_var[:, :, 1], ACT.Sqrt, bias=EPS).then_inc(std_done, 1)
            for i in range(NT):
                act.wait_ge(x1_tr, i + 1)
                if i >= 4:
                    act.wait_ge(ffn_done, i - 3)
                sca.activation(x1T[:, i % 4, :], (pj_ps, o_ps)[i % 2][:, 0:P], ACT.Copy).then_inc(x1T_out, 1)
            act.wait_ge(var_done, 2 * NT)
            sca.activation(std, mean_var[:, :, 1], ACT.Sqrt, bias=EPS).then_inc(std_done, 1)


def kernel(L0_attn_x, L0_attn_qkv_w, L0_attn_out_w, L0_attn_bias_p, L0_attn_bias_a, L0_attn_rope_freqs,
           L0_ffn_weight):
    import concourse.bacc as bacc
    from concourse.bass_utils import run_bass_kernel_spmd

    x = np.asarray(L0_attn_x)
    arrays = {
        "xT": np.ascontiguousarray(x[0].T),
        "x": np.ascontiguousarray(x),
        "wqkvT": np.ascontiguousarray(np.asarray(L0_attn_qkv_w).reshape(3, H * D, DM).transpose(2, 0, 1)),
        "owT": np.ascontiguousarray(np.tile(np.asarray(L0_attn_out_w).reshape(DM, H, D).transpose(1, 2, 0), (1, 2, 1))),
        "bias_p": np.ascontiguousarray(np.asarray(L0_attn_bias_p).reshape(H, 1)),
        "bias_a": np.ascontiguousarray(np.asarray(L0_attn_bias_a).reshape(H, 1)),
        "freqs": np.ascontiguousarray(np.tile(np.asarray(L0_attn_rope_freqs).reshape(D // 2, 1), (4, 1))),
        "ffnT": np.ascontiguousarray(np.asarray(L0_ffn_weight).T),
    }
    nc = bacc.Bacc("TRN2", target_bir_lowering=False, num_devices=1)
    args = [nc.dram_tensor(n, a.shape, mybir.dt.from_np(a.dtype), kind="ExternalInput").ap()
            for n, a in arrays.items()]
    out = nc.dram_tensor("out", (1, S, DM), F32, kind="ExternalOutput").ap()
    rows = nc.dram_tensor("rows", (H, ROW), F32, kind="Internal").ap()
    layer(nc, *args, out, rows)
    return run_bass_kernel_spmd(nc, [arrays], core_ids=[0]).results[0]["out"]
```
